# Optimizing a Trainium2 kernel written in Bass

```python
import numpy as np
import jax
import jax.numpy as jnp

def _softmax(x, axis=-1):
    return jax.nn.softmax(x, axis=axis)

def _gelu(x):
    return jax.nn.gelu(x, approximate=True)

def _silu(x):
    return jax.nn.silu(x)

def _sigmoid(x):
    return jax.nn.sigmoid(x)

def _layernorm(x, axis=-1, eps=1e-05):
    m = jnp.mean(x, axis=axis, keepdims=True)
    v = jnp.var(x, axis=axis, keepdims=True)
    return (x - m) / jnp.sqrt(v + eps)

def _scatter_add(tgt, idx, src, axis=0):
    return tgt.at[idx].add(src)

def _segment_sum(src, seg, n):
    return jax.ops.segment_sum(src, seg, n)
kernel_name = 'mk_dlrm_tower_d1_rec_r8_786a94'

def setup_inputs(seed: int=0):
    np.random.seed(seed)
    _w = jnp.asarray

    def _rec_inputs():
        import jax
        import jax.numpy as jnp
        _tk = jax.random.key(seed)
        dense_ctx = jax.random.normal(jax.random.fold_in(_tk, 190), (2048, 16), jnp.float32)
        ids = jnp.stack([jax.random.randint(jax.random.fold_in(_tk, 200 + f), (2048,), 0, v, jnp.int32) for f, v in enumerate([12500, 12500, 125000, 12500, 1000, 1250, 1250, 12500, 1250, 12500, 1250, 1250, 12500, 1000, 1250, 12500, 1250, 12500, 1000, 1000, 1250, 1000, 1000, 1000, 1250, 1250, 1250])], axis=1)
        tbl_0 = 0.05 * jax.random.normal(jax.random.fold_in(_tk, 500 + 0), (12500, 128), jnp.float32)
        tbl_1 = 0.05 * jax.random.normal(jax.random.fold_in(_tk, 500 + 1), (12500, 128), jnp.float32)
        tbl_2 = 0.05 * jax.random.normal(jax.random.fold_in(_tk, 500 + 2), (125000, 128), jnp.float32)
        tbl_3 = 0.05 * jax.random.normal(jax.random.fold_in(_tk, 500 + 3), (12500, 128), jnp.float32)
        tbl_4 = 0.05 * jax.random.normal(jax.random.fold_in(_tk, 500 + 4), (1000, 128), jnp.float32)
        tbl_5 = 0.05 * jax.random.normal(jax.random.fold_in(_tk, 500 + 5), (1250, 128), jnp.float32)
        tbl_6 = 0.05 * jax.random.normal(jax.random.fold_in(_tk, 500 + 6), (1250, 128), jnp.float32)
        tbl_7 = 0.05 * jax.random.normal(jax.random.fold_in(_tk, 500 + 7), (12500, 128), jnp.float32)
        tbl_8 = 0.05 * jax.random.normal(jax.random.fold_in(_tk, 500 + 8), (1250, 128), jnp.float32)
        tbl_9 = 0.05 * jax.random.normal(jax.random.fold_in(_tk, 500 + 9), (12500, 128), jnp.float32)
        tbl_10 = 0.05 * jax.random.normal(jax.random.fold_in(_tk, 500 + 10), (1250, 128), jnp.float32)
        tbl_11 = 0.05 * jax.random.normal(jax.random.fold_in(_tk, 500 + 11), (1250, 128), jnp.float32)
        tbl_12 = 0.05 * jax.random.normal(jax.random.fold_in(_tk, 500 + 12), (12500, 128), jnp.float32)
        tbl_13 = 0.05 * jax.random.normal(jax.random.fold_in(_tk, 500 + 13), (1000, 128), jnp.float32)
        tbl_14 = 0.05 * jax.random.normal(jax.random.fold_in(_tk, 500 + 14), (1250, 128), jnp.float32)
        tbl_15 = 0.05 * jax.random.normal(jax.random.fold_in(_tk, 500 + 15), (12500, 128), jnp.float32)
        tbl_16 = 0.05 * jax.random.normal(jax.random.fold_in(_tk, 500 + 16), (1250, 128), jnp.float32)
        tbl_17 = 0.05 * jax.random.normal(jax.random.fold_in(_tk, 500 + 17), (12500, 128), jnp.float32)
        tbl_18 = 0.05 * jax.random.normal(jax.random.fold_in(_tk, 500 + 18), (1000, 128), jnp.float32)
        tbl_19 = 0.05 * jax.random.normal(jax.random.fold_in(_tk, 500 + 19), (1000, 128), jnp.float32)
        tbl_20 = 0.05 * jax.random.normal(jax.random.fold_in(_tk, 500 + 20), (1250, 128), jnp.float32)
        tbl_21 = 0.05 * jax.random.normal(jax.random.fold_in(_tk, 500 + 21), (1000, 128), jnp.float32)
        tbl_22 = 0.05 * jax.random.normal(jax.random.fold_in(_tk, 500 + 22), (1000, 128), jnp.float32)
        tbl_23 = 0.05 * jax.random.normal(jax.random.fold_in(_tk, 500 + 23), (1000, 128), jnp.float32)
        tbl_24 = 0.05 * jax.random.normal(jax.random.fold_in(_tk, 500 + 24), (1250, 128), jnp.float32)
        tbl_25 = 0.05 * jax.random.normal(jax.random.fold_in(_tk, 500 + 25), (1250, 128), jnp.float32)
        tbl_26 = 0.05 * jax.random.normal(jax.random.fold_in(_tk, 500 + 26), (1250, 128), jnp.float32)
        _rk = jax.random.fold_in(_tk, 7)
        W_top1 = 0.0521996 * jax.random.normal(jax.random.fold_in(_tk, 801), (367, 512), jnp.float32)
        W_top2 = 0.0441942 * jax.random.normal(jax.random.fold_in(_tk, 802), (512, 256), jnp.float32)
        W_top3 = 0.0625 * jax.random.normal(jax.random.fold_in(_tk, 803), (256, 1), jnp.float32)
        b_top1 = jnp.zeros((512,), jnp.float32)
        b_top2 = jnp.zeros((256,), jnp.float32)
        return (dense_ctx, ids, tbl_0, tbl_1, tbl_2, tbl_3, tbl_4, tbl_5, tbl_6, tbl_7, tbl_8, tbl_9, tbl_10, tbl_11, tbl_12, tbl_13, tbl_14, tbl_15, tbl_16, tbl_17, tbl_18, tbl_19, tbl_20, tbl_21, tbl_22, tbl_23, tbl_24, tbl_25, tbl_26, W_top1, b_top1, W_top2, b_top2, W_top3)
    dense_ctx, ids, tbl_0, tbl_1, tbl_2, tbl_3, tbl_4, tbl_5, tbl_6, tbl_7, tbl_8, tbl_9, tbl_10, tbl_11, tbl_12, tbl_13, tbl_14, tbl_15, tbl_16, tbl_17, tbl_18, tbl_19, tbl_20, tbl_21, tbl_22, tbl_23, tbl_24, tbl_25, tbl_26, W_top1, b_top1, W_top2, b_top2, W_top3 = _rec_inputs()

    def _L0_rec_setup():
        import jax, jax.numpy as jnp
        import numpy as np

        def _tri_indices(num_feas):
            return np.array([i * num_feas + j for j in range(1, num_feas) for i in range(j)], dtype=np.int32)
        key = jax.random.key(seed)
        batch, num_feas, embed_dim = (2048, 27, 128)
        inputs = jax.random.normal(key, (batch, num_feas, embed_dim), dtype=jnp.float32)
        return {'inputs': inputs, 'num_feas': num_feas}
    _L0_rec_all = _L0_rec_setup()
    _L0_rec_in = {k: v for k, v in _L0_rec_all.items() if k in ()}
    del _L0_rec_all
    return {'dense_ctx': dense_ctx, 'ids': ids, 'tbl_0': tbl_0, 'tbl_1': tbl_1, 'tbl_2': tbl_2, 'tbl_3': tbl_3, 'tbl_4': tbl_4, 'tbl_5': tbl_5, 'tbl_6': tbl_6, 'tbl_7': tbl_7, 'tbl_8': tbl_8, 'tbl_9': tbl_9, 'tbl_10': tbl_10, 'tbl_11': tbl_11, 'tbl_12': tbl_12, 'tbl_13': tbl_13, 'tbl_14': tbl_14, 'tbl_15': tbl_15, 'tbl_16': tbl_16, 'tbl_17': tbl_17, 'tbl_18': tbl_18, 'tbl_19': tbl_19, 'tbl_20': tbl_20, 'tbl_21': tbl_21, 'tbl_22': tbl_22, 'tbl_23': tbl_23, 'tbl_24': tbl_24, 'tbl_25': tbl_25, 'tbl_26': tbl_26, 'W_top1': W_top1, 'b_top1': b_top1, 'W_top2': W_top2, 'b_top2': b_top2, 'W_top3': W_top3}

def reference(dense_ctx, ids, tbl_0, tbl_1, tbl_2, tbl_3, tbl_4, tbl_5, tbl_6, tbl_7, tbl_8, tbl_9, tbl_10, tbl_11, tbl_12, tbl_13, tbl_14, tbl_15, tbl_16, tbl_17, tbl_18, tbl_19, tbl_20, tbl_21, tbl_22, tbl_23, tbl_24, tbl_25, tbl_26, W_top1, b_top1, W_top2, b_top2, W_top3):
    import jax
    import jax.numpy as jnp

    def _L0_rec_ref(inputs, num_feas):
        import jax, jax.numpy as jnp
        import numpy as np

        def _tri_indices(num_feas):
            return np.array([i * num_feas + j for j in range(1, num_feas) for i in range(j)], dtype=np.int32)
        dot = jnp.einsum('bnd,bmd->bnm', inputs, inputs)
        idx = jnp.asarray(_tri_indices(num_feas))
        flat = dot.reshape(inputs.shape[0], num_feas * num_feas)
        return flat[:, idx]
    e = jnp.stack([tbl_0[ids[:, 0]], tbl_1[ids[:, 1]], tbl_2[ids[:, 2]], tbl_3[ids[:, 3]], tbl_4[ids[:, 4]], tbl_5[ids[:, 5]], tbl_6[ids[:, 6]], tbl_7[ids[:, 7]], tbl_8[ids[:, 8]], tbl_9[ids[:, 9]], tbl_10[ids[:, 10]], tbl_11[ids[:, 11]], tbl_12[ids[:, 12]], tbl_13[ids[:, 13]], tbl_14[ids[:, 14]], tbl_15[ids[:, 15]], tbl_16[ids[:, 16]], tbl_17[ids[:, 17]], tbl_18[ids[:, 18]], tbl_19[ids[:, 19]], tbl_20[ids[:, 20]], tbl_21[ids[:, 21]], tbl_22[ids[:, 22]], tbl_23[ids[:, 23]], tbl_24[ids[:, 24]], tbl_25[ids[:, 25]], tbl_26[ids[:, 26]]], axis=1)
    z = _L0_rec_ref(e, 27)
    z = z.reshape(z.shape[0], -1)
    h = jnp.concatenate([z, dense_ctx], axis=1)
    h = jnp.maximum(h @ W_top1 + b_top1, 0.0)
    h = jnp.maximum(h @ W_top2 + b_top2, 0.0)
    y = h @ W_top3
    return y

_drawn_inputs = setup_inputs


def setup_inputs(seed=0):
    import zlib

    import numpy as np

    out = dict(_drawn_inputs(seed))
    spreads = {'b_top1': (0.0, 0.1), 'b_top2': (0.0, 0.1)}
    factors = {}
    for name, (base, spread) in spreads.items():
        noise = np.random.default_rng([zlib.crc32(name.encode()), seed]).standard_normal(out[name].shape)
        drawn = base * np.exp(spread * noise) if base else spread * noise
        out[name] = jnp.asarray(drawn.astype(out[name].dtype))
    for name, factor in factors.items():
        out[name] = (out[name] * factor).astype(out[name].dtype)
    return out
```

```python
from contextlib import ExitStack

import concourse.bass as bass
from concourse import mybir

P = 128
F32 = mybir.dt.float32
I32 = mybir.dt.int32
ALU = mybir.AluOpType
ACT = mybir.ActivationFunctionType


def dlrm_tower(nc, dense, ids, tables, w1, b1, w2, b2, w3, y):
    B, FEATS = ids.shape
    D = tables[0].shape[1]
    DENSE = dense.shape[1]
    H1, H2 = w2.shape
    FLAT = w1.shape[0]
    PAIRS = FEATS * (FEATS - 1) // 2
    assert D == P and FLAT == PAIRS + DENSE

    TILE = P
    TT = 4
    BLOCK = TILE * TT
    BLOCKS = B // BLOCK
    ROWS = 32
    J = P // ROWS
    G = BLOCK // J
    GT = TILE // J
    N = FEATS - 1
    PER_BANK = 4
    QUADS = -(-FEATS // PER_BANK)
    UNIT = 2 * PER_BANK
    UNITS = GT // UNIT
    ZB = -(-N // PER_BANK)
    KC = -(-FLAT // P)
    C1 = H1 // P
    C2 = H2 // P

    def quad(q):
        return range(q * PER_BANK, min(FEATS, (q + 1) * PER_BANK))

    ctx = ExitStack()
    with ctx:
        def sb(name, shape, dt=F32):
            return ctx.enter_context(nc.sbuf_tensor(name, shape, dt))

        def ps(name, shape):
            return ctx.enter_context(nc.psum_tensor(name, shape, F32))

        def sem(name):
            return ctx.enter_context(nc.semaphore(name))

        idx = sb("idx", [P, TT, FEATS], I32)
        emb = sb("emb", [P, 2, FEATS, D])
        embT = sb("embT", [P, 2, TILE, ROWS])
        gram = sb("gram", [P, N, G])
        flat = sb("flat", [P, J, FLAT])
        flatT = sb("flatT", [P, KC, BLOCK])
        h1T = sb("h1T", [P, C1, BLOCK])
        h2T = sb("h2T", [P, C2, BLOCK])
        y_sb = sb("y_sb", [1, 2, BLOCK])
        w1_sb = sb("w1_sb", [P, KC, H1])
        w2_sb = sb("w2_sb", [P, C1, H2])
        w3_sb = sb("w3_sb", [P, C2])
        b1_sb = sb("b1_sb", [P, C1])
        b2_sb = sb("b2_sb", [P, C2])
        ident = sb("ident", [P, P])

        turn_ps = [ps(f"turn_ps{i}", [P, 512]) for i in range(2)]
        gram_ps = [ps(f"gram_ps{i}", [P, 2, 512]) for i in range(2)]
        late_ps = [ps(f"late_ps{i}", [P, 512]) for i in range(2)]

        ident_zeroed = sem("ident_zeroed")
        ident_ready = sem("ident_ready")
        pad_zeroed = sem("pad_zeroed")
        weights_loaded = sem("weights_loaded")
        idx_loaded = [sem(f"idx_loaded{t}") for t in range(TT)]
        gathered = [[sem(f"gathered{b}_{q}") for q in range(QUADS)] for b in range(2)]
        gather_allowed = sem("gather_allowed")
        turned = sem("turned")
        embT_ready = sem("embT_ready")
        dotted = sem("dotted")
        gram_ready = sem("gram_ready")
        z_turned = sem("z_turned")
        flat_ready = sem("flat_ready")
        dense_loaded = sem("dense_loaded")
        flat_turned = sem("flat_turned")
        flatT_ready = sem("flatT_ready")
        h1_summed = sem("h1_summed")
        h1_ready = sem("h1_ready")
        h2_summed = sem("h2_summed")
        h2_ready = sem("h2_ready")
        y_summed = sem("y_summed")
        y_ready = sem("y_ready")
        y_stored = [sem(f"y_stored{i}") for i in range(2)]

        block = ctx.enter_context(nc.Block())

        def each_block(eng, body):
            body(0)
            with eng.Fori(1, BLOCKS) as s:
                body(s)

        def first(s):
            return isinstance(s, int) and s == 0

        @block.sync
        def _(sp):
            for t in range(TT):
                sp.dma_start(idx[:, t, :], ids[t * TILE:(t + 1) * TILE, :]).then_inc(idx_loaded[t], 16)
            for k in range(KC):
                rows = min(P, FLAT - k * P)
                sp.dma_start(w1_sb[0:rows, k, :], w1[k * P:k * P + rows, :]).then_inc(weights_loaded, 16)
            sp.dma_start(w2_sb[:, :, :], w2.rearrange("(k p) n -> p k n", p=P)).then_inc(weights_loaded, 16)
            sp.dma_start(w3_sb[:, :], w3).then_inc(weights_loaded, 16)
            sp.dma_start(b1_sb[:, :], b1).then_inc(weights_loaded, 16)
            sp.dma_start(b2_sb[:, :], b2).then_inc(weights_loaded, 16)

            def load_dense(s):
                src = dense[bass.ds(s * BLOCK, BLOCK), :].rearrange("(g j) f -> g j f", j=J)
                sp.dma_start(flat[:, :, PAIRS:FLAT], src).then_inc(dense_loaded, 16)

            load_dense(0)
            with sp.Fori(1, BLOCKS) as s:
                for t in range(TT):
                    sp.wait_ge(turned, QUADS * (TT * (s - 1) + t + 1))
                    sp.dma_start(idx[:, t, :], ids[bass.ds(s * BLOCK + t * TILE, TILE), :]).then_inc(idx_loaded[t], 16)
                sp.wait_ge(flat_turned, KC * s)
                load_dense(s)

        @block.gpsimd
        def _(pool):
            pool.memset(ident[:, :], 0.0).then_inc(ident_zeroed, 1)
            pool.wait_ge(ident_zeroed, 1)
            pool.affine_select(out=ident[:, :], in_=ident[:, :], compare_op=ALU.not_equal, fill=1.0, base=0,
                               pattern=[[-1, P]], channel_multiplier=1).then_inc(ident_ready, 1)

            def gathers(s):
                for t in range(TT):
                    pool.wait_ge(idx_loaded[t], 16 * (s + 1))
                    for q in range(QUADS):
                        if not (first(s) and t < 2):
                            pool.wait_ge(turned, QUADS * (TT * s + t - 2) + q + 1)
                        pool.sem_inc(gather_allowed, 1)
                        for f in quad(q):
                            pool.indirect_dma_start(
                                emb[:, t % 2, f, :], None, tables[f][:, :],
                                bass.IndirectOffsetOnAxis(ap=idx[:, t, f:f + 1], axis=0),
                            ).then_inc(gathered[t % 2][q], 16)

            each_block(pool, gathers)

        @block.tensor
        def _(pe):
            pe.wait_ge(ident_ready, 1)
            pe.wait_ge(weights_loaded, 16 * (KC + 4))
            pe.wait_ge(pad_zeroed, 2)

            def turn(s, t):
                for q in range(QUADS):
                    k = t * QUADS + q
                    pe.wait_ge(gathered[t % 2][q], 16 * len(quad(q)) * (2 * s + t // 2 + 1))
                    if not (first(s) and k < 2):
                        pe.wait_ge(embT_ready, QUADS * TT * s + k - 1)
                    for i, f in enumerate(quad(q)):
                        last = pe.transpose(turn_ps[k % 2][:, i * P:(i + 1) * P], emb[:, t % 2, f, :], ident[:, :])
                    last.then_inc(turned, 1)

            def dots(s, t):
                pe.wait_ge(embT_ready, QUADS * (TT * s + t + 1))
                for u in range(UNITS):
                    if not (first(s) and t == 0 and u < 2):
                        pe.wait_ge(gram_ready, UNITS * (TT * s + t) + u - 1)
                    for i in range(UNIT):
                        c = (u * UNIT + i) * J
                        o = gram_ps[u % 2][:, i // PER_BANK, (i % PER_BANK) * J * N:(i % PER_BANK + 1) * J * N]
                        last = pe.matmul(o, embT[:, t % 2, c:c + J, :], embT[:, t % 2, c:c + J, 1:FEATS],
                                         start=True, stop=True)
                    last.then_inc(dotted, 1)

            def turn_dots(s):
                pe.wait_ge(gram_ready, UNITS * TT * (s + 1))
                if not first(s):
                    pe.wait_ge(y_ready, s)
                for z in range(ZB):
                    if z >= 2:
                        pe.wait_ge(flat_ready, ZB * s + z - 1)
                    for i, n in enumerate(range(z * PER_BANK, min(N, (z + 1) * PER_BANK))):
                        last = pe.transpose(late_ps[z % 2][:, i * P:(i + 1) * P], gram[:, n, :], ident[:, :])
                    last.then_inc(z_turned, 1)

            def turn_flat(s):
                pe.wait_ge(flat_ready, ZB * (s + 1))
                pe.wait_ge(dense_loaded, 16 * (s + 1))
                for k in range(KC):
                    rows = min(P, FLAT - k * P)
                    if k >= 2:
                        pe.wait_ge(flatT_ready, KC * s + k - 1)
                    for j in range(J):
                        last = pe.transpose(late_ps[(ZB + k) % 2][0:rows, j * P:(j + 1) * P],
                                            flat[:, j, k * P:k * P + rows], ident[:, :])
                    last.then_inc(flat_turned, 1)

            def layer1(s):
                pe.wait_ge(flatT_ready, KC * (s + 1))
                for c in range(C1):
                    if c >= 2:
                        pe.wait_ge(h1_ready, C1 * s + c - 1)
                    for k in range(KC):
                        rows = min(P, FLAT - k * P)
                        last = pe.matmul(late_ps[(ZB + KC + c) % 2][:, :], w1_sb[0:rows, k, c * P:(c + 1) * P],
                                         flatT[0:rows, k, :], start=(k == 0), stop=(k == KC - 1))
                    last.then_inc(h1_summed, 1)

            def layer2(s):
                pe.wait_ge(h1_ready, C1 * (s + 1))
                for c in range(C2):
                    for k in range(C1):
                        last = pe.matmul(late_ps[(ZB + KC + C1 + c) % 2][:, :], w2_sb[:, k, c * P:(c + 1) * P],
                                         h1T[:, k, :], start=(k == 0), stop=(k == C1 - 1))
                    last.then_inc(h2_summed, 1)

            def layer3(s):
                pe.wait_ge(h2_ready, C2 * (s + 1))
                for k in range(C2):
                    last = pe.matmul(late_ps[(ZB + KC + C1 + C2) % 2][0:1, :], w3_sb[:, k:k + 1], h2T[:, k, :],
                                     start=(k == 0), stop=(k == C2 - 1))
                last.then_inc(y_summed, 1)

            def body(s):
                turn(s, 0)
                if not first(s):
                    turn_dots(s - 1)
                dots(s, 0)
                turn(s, 1)
                if not first(s):
                    turn_flat(s - 1)
                    layer1(s - 1)
                dots(s, 1)
                turn(s, 2)
                if not first(s):
                    layer2(s - 1)
                dots(s, 2)
                turn(s, 3)
                if not first(s):
                    layer3(s - 1)
                dots(s, 3)

            each_block(pe, body)
            turn_dots(BLOCKS - 1)
            turn_flat(BLOCKS - 1)
            layer1(BLOCKS - 1)
            layer2(BLOCKS - 1)
            layer3(BLOCKS - 1)

        @block.vector
        def _(dve):
            for b in range(2):
                dve.memset(embT[:, b, :, FEATS:ROWS], 0.0).then_inc(pad_zeroed, 1)

            def copy_turned(s, t):
                if not (first(s) and t < 2):
                    dve.wait_ge(dotted, UNITS * (TT * s + t - 1))
                for q in range(QUADS):
                    k = t * QUADS + q
                    n = len(quad(q))
                    dve.wait_ge(turned, QUADS * TT * s + k + 1)
                    dve.tensor_copy(
                        embT[:, t % 2, :, q * PER_BANK:q * PER_BANK + n].rearrange("p c f -> p f c"),
                        turn_ps[k % 2][:, 0:n * P].rearrange("p (f c) -> p f c", f=n),
                    ).then_inc(embT_ready, 1)

            def copy_dots(s):
                if not first(s):
                    dve.wait_ge(flat_turned, KC * s)
                for z in range(ZB):
                    dve.wait_ge(z_turned, ZB * s + z + 1)
                    for i, n in enumerate(range(z * PER_BANK + 1, min(N, (z + 1) * PER_BANK) + 1)):
                        at = n * (n - 1) // 2
                        last = dve.tensor_copy(
                            flat[:, :, at:at + n],
                            late_ps[z % 2][:, i * P:(i + 1) * P].rearrange("p (j m) -> p j m", j=J)[:, :, 0:n])
                    last.then_inc(flat_ready, 1)

            def body(s):
                copy_turned(s, 0)
                if not first(s):
                    copy_dots(s - 1)
                for t in range(1, TT):
                    copy_turned(s, t)

            each_block(dve, body)
            copy_dots(BLOCKS - 1)

        @block.scalar
        def _(act):
            def copy_gram(s, t):
                if t == 0 and not first(s):
                    act.wait_ge(z_turned, ZB * s)
                for u in range(UNITS):
                    act.wait_ge(dotted, UNITS * (TT * s + t) + u + 1)
                    g = t * GT + u * UNIT
                    for j in range(J):
                        rows = slice(j * ROWS, (j + 1) * ROWS)
                        src = gram_ps[u % 2][rows, :, 0:PER_BANK * J * N].rearrange(
                            "p b (g j n) -> p b g j n", g=PER_BANK, j=J)[:, :, :, j, :]
                        dst = gram[rows, :, g:g + UNIT].rearrange("p n (b g) -> p b g n", b=2)
                        last = act.copy(dst, src)
                    last.then_inc(gram_ready, 1)

            def copy_flat(s):
                for k in range(KC):
                    rows = min(P, FLAT - k * P)
                    act.wait_ge(flat_turned, KC * s + k + 1)
                    act.copy(flatT[0:rows, k, :], late_ps[(ZB + k) % 2][0:rows, :]).then_inc(flatT_ready, 1)

            def relu1(s):
                for c in range(C1):
                    act.wait_ge(h1_summed, C1 * s + c + 1)
                    act.activation(h1T[:, c, :], late_ps[(ZB + KC + c) % 2][:, :], ACT.Relu,
                                   bias=b1_sb[:, c:c + 1]).then_inc(h1_ready, 1)

            def relu2(s):
                for c in range(C2):
                    act.wait_ge(h2_summed, C2 * s + c + 1)
                    act.activation(h2T[:, c, :], late_ps[(ZB + KC + C1 + c) % 2][:, :], ACT.Relu,
                                   bias=b2_sb[:, c:c + 1]).then_inc(h2_ready, 1)

            def store(s, slot):
                act.wait_ge(y_summed, s + 1)
                act.copy(y_sb[0:1, slot, :].rearrange("a (g j) -> a j g", j=J),
                         late_ps[(ZB + KC + C1 + C2) % 2][0:1, :].rearrange("a (j g) -> a j g", j=J),
                         ).then_inc(y_ready, 1)
                act.wait_ge(y_ready, s + 1)
                act.dma_start(y[bass.ds(s * BLOCK, BLOCK), :].rearrange("n a -> a n"),
                              y_sb[0:1, slot, :]).then_inc(y_stored[slot], 16)

            def body(s):
                copy_gram(s, 0)
                if not first(s):
                    copy_flat(s - 1)
                    relu1(s - 1)
                copy_gram(s, 1)
                if not first(s):
                    relu2(s - 1)
                copy_gram(s, 2)
                if not first(s):
                    if not isinstance(s, int):
                        act.wait_ge(y_stored[0], 16 * (s - 1))
                    store(s - 1, 0)
                copy_gram(s, 3)

            act.wait_ge(weights_loaded, 16 * (KC + 4))
            each_block(act, body)
            copy_flat(BLOCKS - 1)
            relu1(BLOCKS - 1)
            relu2(BLOCKS - 1)
            store(BLOCKS - 1, 1)
            act.wait_ge(y_stored[0], 16 * (BLOCKS - 1))
            act.wait_ge(y_stored[1], 16)


def kernel(**inputs):
    import numpy as np
    import concourse.bacc as bacc
    from concourse.bass_utils import run_bass_kernel_spmd

    arrays = {name: np.ascontiguousarray(a) for name, a in inputs.items()}
    for name in ("b_top1", "b_top2", "W_top3"):
        arrays[name] = np.ascontiguousarray(arrays[name].reshape(-1, P).T)
    nc = bacc.Bacc("TRN2", target_bir_lowering=False, num_devices=1)
    ap = {name: nc.dram_tensor(f"in_{name}", a.shape, mybir.dt.from_np(a.dtype), kind="ExternalInput").ap()
          for name, a in arrays.items()}
    feats = arrays["ids"].shape[1]
    y = nc.dram_tensor("out_y", (arrays["ids"].shape[0], 1), F32, kind="ExternalOutput").ap()
    dlrm_tower(nc, ap["dense_ctx"], ap["ids"], [ap[f"tbl_{f}"] for f in range(feats)], ap["W_top1"], ap["b_top1"],
               ap["W_top2"], ap["b_top2"], ap["W_top3"], y)
    r = run_bass_kernel_spmd(nc, [{f"in_{name}": a for name, a in arrays.items()}], core_ids=[0])
    return r.results[0]["out_y"]
```

```python
from contextlib import ExitStack

import concourse.bass as bass
from concourse import mybir

P = 128
F32 = mybir.dt.float32
F32R = mybir.dt.float32r
I32 = mybir.dt.int32
ONE_HOT = (4, 13, 18, 19, 20, 21, 22, 23, 24)
ROWS_PER_CHUNK = 125
ALU = mybir.AluOpType
ACT = mybir.ActivationFunctionType


def dlrm_tower(nc, dense, ids, idsT, tables, w1, b1, w2, b2, w3, y):
    B, FEATS = ids.shape
    D = tables[0].shape[1]
    DENSE = dense.shape[1]
    H1, H2 = w2.shape
    FLAT = w1.shape[0]
    PAIRS = FEATS * (FEATS - 1) // 2
    assert D == P and FLAT == PAIRS + DENSE

    TILE = P
    TT = 4
    BLOCK = TILE * TT
    BLOCKS = B // BLOCK
    ROWS = 32
    J = P // ROWS
    G = BLOCK // J
    GT = TILE // J
    N = FEATS - 1
    PER_BANK = 4
    GATHERED = [f for f in range(FEATS) if f not in ONE_HOT]
    GF = len(GATHERED)
    QUADS = -(-GF // PER_BANK)
    HALF = BLOCK // 2
    HT = HALF // TILE
    O = len(ONE_HOT)
    R = ROWS_PER_CHUNK
    CHUNKS = [tables[f].shape[0] // R for f in ONE_HOT]
    MAXC = max(CHUNKS)
    GROUP = MAXC // 2
    SLOTS = 4
    GH = 2 * O
    O_FIRST = (O + 1) // 2
    STEPS = O + HT * QUADS
    STAGES = 4
    assert all(tables[f].shape[0] == R * c and c % 2 == 0 for f, c in zip(ONE_HOT, CHUNKS))
    assert 2 * GH % SLOTS == 0 and 2 * STEPS % 2 == 0
    UNIT = 2 * PER_BANK
    UNITS = GT // UNIT
    ZB = -(-N // PER_BANK)
    KC = -(-FLAT // P)
    C1 = H1 // P
    C2 = H2 // P

    def quad(q):
        return GATHERED[q * PER_BANK:(q + 1) * PER_BANK]

    assert all(quad(q)[-1] - quad(q)[0] == len(quad(q)) - 1 for q in range(QUADS))

    def group_chunks(o, i):
        return range(i * CHUNKS[o] // 2, (i + 1) * CHUNKS[o] // 2)

    def one_hot_step(o):
        return o if o < O_FIRST else o + QUADS

    def quad_step(t, q):
        return O_FIRST + q if t == 0 else O + QUADS + q

    ctx = ExitStack()
    with ctx:
        def sb(name, shape, dt=F32):
            return ctx.enter_context(nc.sbuf_tensor(name, shape, dt))

        def ps(name, shape):
            return ctx.enter_context(nc.psum_tensor(name, shape, F32))

        def sem(name):
            return ctx.enter_context(nc.semaphore(name))

        idx = sb("idx", [P, TT, FEATS], I32)
        emb = sb("emb", [P, 2, GF, D])
        tbl_parts = sb("tbl_parts", [R, 2, sum(CHUNKS), D], F32R)
        ids_rows = sb("ids_rows", [R, O, HALF], I32)
        one_hot = sb("one_hot", [R, SLOTS, GROUP, HALF], F32R)
        row_i = sb("row_i", [R, MAXC], I32)
        row_of = sb("row_of", [R, MAXC])
        embT = sb("embT", [P, 2, TILE, ROWS])
        gram = sb("gram", [P, N, G])
        flat = sb("flat", [P, J, FLAT])
        flatT = sb("flatT", [P, KC, BLOCK])
        h1T = sb("h1T", [P, C1, BLOCK])
        h2T = sb("h2T", [P, C2, BLOCK])
        y_sb = sb("y_sb", [1, BLOCK])
        w1_sb = sb("w1_sb", [P, KC, H1])
        w2_sb = sb("w2_sb", [P, C1, H2])
        w3_sb = sb("w3_sb", [P, C2])
        b1_sb = sb("b1_sb", [P, C1])
        b2_sb = sb("b2_sb", [P, C2])
        ident = sb("ident", [P, P])

        gram_flat = gram[0:R, :, :].rearrange("p n g -> p (n g)")
        stage = [gram_flat[:, 0:MAXC * D], gram_flat[:, MAXC * D:2 * MAXC * D],
                 h1T[0:R, :, :].rearrange("p c n -> p (c n)")[:, 0:MAXC * D],
                 flatT[0:R, :, :].rearrange("p c n -> p (c n)")[:, 0:MAXC * D]]
        part_at = [sum(CHUNKS[:o]) for o in range(O)]

        embT_ps = [ps(f"embT_ps{i}", [P, 512]) for i in range(2)]
        gram_ps = [ps(f"gram_ps{i}", [P, 2, 512]) for i in range(2)]
        late_ps = [ps(f"late_ps{i}", [P, 512]) for i in range(2)]

        ident_zeroed = sem("ident_zeroed")
        ident_ready = sem("ident_ready")
        pad_zeroed = sem("pad_zeroed")
        weights_loaded = sem("weights_loaded")
        idx_loaded = [sem(f"idx_loaded{t}") for t in range(TT)]
        gathered = [[sem(f"gathered{b}_{q}") for q in range(QUADS)] for b in range(2)]
        gather_allowed = sem("gather_allowed")
        turned = sem("turned")
        rows_numbered = sem("rows_numbered")
        row_of_ready = sem("row_of_ready")
        staged = [sem(f"staged{i}") for i in range(STAGES)]
        high_ready = sem("high_ready")
        low_ready = sem("low_ready")
        ids_loaded = [sem(f"ids_loaded{o}") for o in range(O)]
        one_hot_built = sem("one_hot_built")
        one_hot_used = sem("one_hot_used")
        embT_ready = sem("embT_ready")
        dotted = sem("dotted")
        gram_ready = sem("gram_ready")
        z_turned = sem("z_turned")
        flat_ready = sem("flat_ready")
        dense_loaded = sem("dense_loaded")
        flat_turned = sem("flat_turned")
        flatT_ready = sem("flatT_ready")
        h1_summed = sem("h1_summed")
        h1_ready = sem("h1_ready")
        h2_summed = sem("h2_summed")
        h2_ready = sem("h2_ready")
        y_summed = sem("y_summed")
        y_ready = sem("y_ready")
        y_stored = sem("y_stored")

        block = ctx.enter_context(nc.Block())

        def each_block(eng, body):
            body(0)
            with eng.Fori(1, BLOCKS) as s:
                body(s)

        def first(s):
            return isinstance(s, int) and s == 0

        @block.sync
        def _(sp):
            def load_idx(s, t):
                if not first(s):
                    sp.wait_ge(turned, QUADS * (TT * (s - 1) + t + 1))
                sp.dma_start(idx[:, t, :], ids[bass.ds(s * BLOCK + t * TILE, TILE), :]).then_inc(idx_loaded[t], 16)

            def load_ids(s, half):
                for o, f in enumerate(ONE_HOT):
                    if not (first(s) and half == 0):
                        sp.wait_ge(one_hot_built, GH * (2 * s + half - 1) + 2 * (o + 1))
                    src = idsT[f:f + 1, bass.ds(s * BLOCK + half * HALF, HALF)].to_broadcast([R, HALF])
                    sp.dma_start(ids_rows[:, o, :], src).then_inc(ids_loaded[o], 16)

            def load_dense(s):
                if not first(s):
                    sp.wait_ge(flat_turned, KC * s)
                src = dense[bass.ds(s * BLOCK, BLOCK), :].rearrange("(g j) f -> g j f", j=J)
                sp.dma_start(flat[:, :, PAIRS:FLAT], src).then_inc(dense_loaded, 16)

            load_idx(0, 0)
            load_ids(0, 0)
            for t in range(1, TT):
                load_idx(0, t)
            for k in range(KC):
                rows = min(P, FLAT - k * P)
                sp.dma_start(w1_sb[0:rows, k, :], w1[k * P:k * P + rows, :]).then_inc(weights_loaded, 16)
            sp.dma_start(w2_sb[:, :, :], w2.rearrange("(k p) n -> p k n", p=P)).then_inc(weights_loaded, 16)
            sp.dma_start(w3_sb[:, :], w3).then_inc(weights_loaded, 16)
            sp.dma_start(b1_sb[:, :], b1).then_inc(weights_loaded, 16)
            sp.dma_start(b2_sb[:, :], b2).then_inc(weights_loaded, 16)
            load_dense(0)
            load_ids(0, 1)
            with sp.Fori(1, BLOCKS) as s:
                for half in range(2):
                    for t in range(half * HT, (half + 1) * HT):
                        load_idx(s, t)
                    load_ids(s, half)
                load_dense(s)

        @block.gpsimd
        def _(pool):
            pool.memset(ident[:, :], 0.0).then_inc(ident_zeroed, 1)
            pool.wait_ge(ident_zeroed, 1)
            pool.affine_select(out=ident[:, :], in_=ident[:, :], compare_op=ALU.not_equal, fill=1.0, base=0,
                               pattern=[[-1, P]], channel_multiplier=1).then_inc(ident_ready, 1)

            pool.iota(row_i[:, :], pattern=[[R, MAXC]], base=0, channel_multiplier=1).then_inc(rows_numbered, 1)

            def gathers(s):
                for t in range(TT):
                    pool.wait_ge(idx_loaded[t], 16 * (s + 1))
                    for q in range(QUADS):
                        if not (first(s) and t < 2):
                            pool.wait_ge(turned, QUADS * (TT * s + t - 2) + q + 1)
                        pool.sem_inc(gather_allowed, 1)
                        for i, f in enumerate(quad(q)):
                            pool.indirect_dma_start(
                                emb[:, t % 2, q * PER_BANK + i, :], None, tables[f][:, :],
                                bass.IndirectOffsetOnAxis(ap=idx[:, t, f:f + 1], axis=0),
                            ).then_inc(gathered[t % 2][q], 16)

            each_block(pool, gathers)

        @block.tensor
        def _(pe):
            pe.wait_ge(ident_ready, 1)
            pe.wait_ge(pad_zeroed, 2)

            def bank_free(s, half, step):
                if not (first(s) and half == 0 and step < 2):
                    pe.wait_ge(embT_ready, STEPS * (2 * s + half) + step - 1)

            def read_one_hot(s, half, o):
                step = one_hot_step(o)
                bank_free(s, half, step)
                out = embT_ps[(half * STEPS + step) % 2][:, 0:HALF]
                if first(s) and half == 0:
                    pe.wait_ge(low_ready, o + 1)
                for i in range(2):
                    k = 2 * o + i
                    pe.wait_ge(one_hot_built, GH * (2 * s + half) + k + 1)
                    for c, chunk in enumerate(group_chunks(o, i)):
                        for part in range(2):
                            last = pe.matmul(out, tbl_parts[:, part, part_at[o] + chunk, :],
                                             one_hot[:, (half * GH + k) % SLOTS, c, :],
                                             start=(chunk == 0 and part == 0),
                                             stop=(chunk == CHUNKS[o] - 1 and part == 1))
                    last.then_inc(one_hot_used, 1)

            def turn(s, t):
                half = t // HT
                for q in range(QUADS):
                    step = quad_step(t % HT, q)
                    pe.wait_ge(gathered[t % 2][q], 16 * len(quad(q)) * (2 * s + t // 2 + 1))
                    bank_free(s, half, step)
                    for i in range(len(quad(q))):
                        last = pe.transpose(embT_ps[(half * STEPS + step) % 2][:, i * P:(i + 1) * P],
                                            emb[:, t % 2, q * PER_BANK + i, :], ident[:, :])
                    last.then_inc(turned, 1)

            def dots(s, t):
                for u in range(UNITS):
                    if not (first(s) and t == 0 and u < 2):
                        pe.wait_ge(gram_ready, UNITS * (TT * s + t) + u - 1)
                    for i in range(UNIT):
                        c = (u * UNIT + i) * J
                        o = gram_ps[u % 2][:, i // PER_BANK, (i % PER_BANK) * J * N:(i % PER_BANK + 1) * J * N]
                        last = pe.matmul(o, embT[:, t % 2, c:c + J, :], embT[:, t % 2, c:c + J, 1:FEATS],
                                         start=True, stop=True)
                    last.then_inc(dotted, 1)

            def turn_dots(s):
                pe.wait_ge(gram_ready, UNITS * TT * (s + 1))
                if not first(s):
                    pe.wait_ge(y_ready, s)
                for z in range(ZB):
                    if z >= 2:
                        pe.wait_ge(flat_ready, ZB * s + z - 1)
                    for i, n in enumerate(range(z * PER_BANK, min(N, (z + 1) * PER_BANK))):
                        last = pe.transpose(late_ps[z % 2][:, i * P:(i + 1) * P], gram[:, n, :], ident[:, :])
                    last.then_inc(z_turned, 1)

            def turn_flat(s):
                pe.wait_ge(flat_ready, ZB * (s + 1))
                pe.wait_ge(dense_loaded, 16 * (s + 1))
                for k in range(KC):
                    rows = min(P, FLAT - k * P)
                    if k >= 2:
                        pe.wait_ge(flatT_ready, KC * s + k - 1)
                    for j in range(J):
                        last = pe.transpose(late_ps[(ZB + k) % 2][0:rows, j * P:(j + 1) * P],
                                            flat[:, j, k * P:k * P + rows], ident[:, :])
                    last.then_inc(flat_turned, 1)

            def layer1(s):
                pe.wait_ge(flatT_ready, KC * (s + 1))
                for c in range(C1):
                    if c >= 2:
                        pe.wait_ge(h1_ready, C1 * s + c - 1)
                    for k in range(KC):
                        rows = min(P, FLAT - k * P)
                        last = pe.matmul(late_ps[(ZB + KC + c) % 2][:, :], w1_sb[0:rows, k, c * P:(c + 1) * P],
                                         flatT[0:rows, k, :], start=(k == 0), stop=(k == KC - 1))
                    last.then_inc(h1_summed, 1)

            def layer2(s):
                pe.wait_ge(h1_ready, C1 * (s + 1))
                for c in range(C2):
                    for k in range(C1):
                        last = pe.matmul(late_ps[(ZB + KC + C1 + c) % 2][:, :], w2_sb[:, k, c * P:(c + 1) * P],
                                         h1T[:, k, :], start=(k == 0), stop=(k == C1 - 1))
                    last.then_inc(h2_summed, 1)

            def layer3(s):
                pe.wait_ge(h2_ready, C2 * (s + 1))
                for k in range(C2):
                    last = pe.matmul(late_ps[(ZB + KC + C1 + C2) % 2][0:1, :], w3_sb[:, k:k + 1], h2T[:, k, :],
                                     start=(k == 0), stop=(k == C2 - 1))
                last.then_inc(y_summed, 1)

            def body(s):
                for half in range(2):
                    for o in range(O_FIRST):
                        read_one_hot(s, half, o)
                    if half == 0 and not first(s):
                        turn_dots(s - 1)
                    turn(s, half * HT)
                    for o in range(O_FIRST, O):
                        read_one_hot(s, half, o)
                    turn(s, half * HT + 1)
                    if not first(s):
                        if half == 0:
                            turn_flat(s - 1)
                        else:
                            layer2(s - 1)
                    pe.wait_ge(embT_ready, STEPS * (2 * s + half + 1))
                    dots(s, half * HT)
                    dots(s, half * HT + 1)
                    if not first(s):
                        if half == 0:
                            layer1(s - 1)
                        else:
                            layer3(s - 1)
                if first(s):
                    pe.wait_ge(weights_loaded, 16 * (KC + 4))

            each_block(pe, body)
            turn_dots(BLOCKS - 1)
            turn_flat(BLOCKS - 1)
            layer1(BLOCKS - 1)
            layer2(BLOCKS - 1)
            layer3(BLOCKS - 1)

        @block.vector
        def _(dve):
            for b in range(2):
                dve.memset(embT[:, b, :, FEATS:ROWS], 0.0).then_inc(pad_zeroed, 1)

            dve.wait_ge(rows_numbered, 1)
            dve.tensor_copy(row_of[:, :], row_i[:, :]).then_inc(row_of_ready, 1)
            dve.wait_ge(row_of_ready, 1)

            def split_low(o):
                at = slice(part_at[o], part_at[o] + CHUNKS[o])
                raw = stage[o % STAGES][:, 0:CHUNKS[o] * D].rearrange("p (c d) -> p c d", d=D)
                dve.wait_ge(high_ready, o + 1)
                dve.tensor_tensor(tbl_parts[:, 1, at, :], raw, tbl_parts[:, 0, at, :].bitcast(F32),
                                  ALU.subtract).then_inc(low_ready, 1)

            def build(s, half, o):
                dve.wait_ge(ids_loaded[o], 16 * (2 * s + half + 1))
                for i in range(2):
                    k = 2 * o + i
                    if not (first(s) and half == 0 and k < SLOTS):
                        dve.wait_ge(one_hot_used, GH * (2 * s + half) + k - SLOTS + 1)
                    for c, chunk in enumerate(group_chunks(o, i)):
                        last = dve.tensor_scalar(one_hot[:, (half * GH + k) % SLOTS, c, :], ids_rows[:, o, :],
                                                 row_of[:, chunk:chunk + 1], None, ALU.is_equal)
                    last.then_inc(one_hot_built, 1)

            def copy_dots(s):
                if not first(s):
                    dve.wait_ge(flat_turned, KC * s)
                for z in range(ZB):
                    dve.wait_ge(z_turned, ZB * s + z + 1)
                    for i, n in enumerate(range(z * PER_BANK + 1, min(N, (z + 1) * PER_BANK) + 1)):
                        at = n * (n - 1) // 2
                        last = dve.tensor_copy(
                            flat[:, :, at:at + n],
                            late_ps[z % 2][:, i * P:(i + 1) * P].rearrange("p (j m) -> p j m", j=J)[:, :, 0:n])
                    last.then_inc(flat_ready, 1)

            def body(s):
                for half in range(2):
                    for o in range(O):
                        if half == 0 and o == O_FIRST and not first(s):
                            copy_dots(s - 1)
                        if first(s) and half == 0:
                            split_low(o)
                        build(s, half, o)

            each_block(dve, body)
            copy_dots(BLOCKS - 1)

        @block.scalar
        def _(act):
            def load_table(o):
                f = ONE_HOT[o]
                act.dma_start(stage[o % STAGES][:, 0:CHUNKS[o] * D].rearrange("p (c d) -> p c d", d=D),
                              tables[f].rearrange("(c p) d -> p c d", p=R)).then_inc(staged[o % STAGES], 16)

            def split_high(o):
                raw = stage[o % STAGES][:, 0:CHUNKS[o] * D].rearrange("p (c d) -> p c d", d=D)
                act.wait_ge(staged[o % STAGES], 16 * (o // STAGES + 1))
                act.copy(tbl_parts[:, 0, part_at[o]:part_at[o] + CHUNKS[o], :], raw).then_inc(high_ready, 1)

            def copy_one_hot(s, half, o):
                step = one_hot_step(o)
                act.wait_ge(one_hot_used, GH * (2 * s + half) + 2 * (o + 1))
                act.copy(embT[:, :, :, ONE_HOT[o]],
                         embT_ps[(half * STEPS + step) % 2][:, 0:HALF].rearrange("p (t c) -> p t c", t=HT),
                         ).then_inc(embT_ready, 1)

            def copy_turned(s, t):
                half = t // HT
                for q in range(QUADS):
                    step = quad_step(t % HT, q)
                    n = len(quad(q))
                    act.wait_ge(turned, QUADS * (TT * s + t) + q + 1)
                    act.copy(
                        embT[:, t % 2, :, quad(q)[0]:quad(q)[0] + n].rearrange("p c f -> p f c"),
                        embT_ps[(half * STEPS + step) % 2][:, 0:n * P].rearrange("p (f c) -> p f c", f=n),
                    ).then_inc(embT_ready, 1)

            def copy_gram(s, t):
                if t == 0 and not first(s):
                    act.wait_ge(z_turned, ZB * s)
                for u in range(UNITS):
                    act.wait_ge(dotted, UNITS * (TT * s + t) + u + 1)
                    g = t * GT + u * UNIT
                    for j in range(J):
                        rows = slice(j * ROWS, (j + 1) * ROWS)
                        src = gram_ps[u % 2][rows, :, 0:PER_BANK * J * N].rearrange(
                            "p b (g j n) -> p b g j n", g=PER_BANK, j=J)[:, :, :, j, :]
                        dst = gram[rows, :, g:g + UNIT].rearrange("p n (b g) -> p b g n", b=2)
                        last = act.copy(dst, src)
                    last.then_inc(gram_ready, 1)

            def copy_flat(s):
                for k in range(KC):
                    rows = min(P, FLAT - k * P)
                    act.wait_ge(flat_turned, KC * s + k + 1)
                    act.copy(flatT[0:rows, k, :], late_ps[(ZB + k) % 2][0:rows, :]).then_inc(flatT_ready, 1)

            def relu1(s):
                for c in range(C1):
                    act.wait_ge(h1_summed, C1 * s + c + 1)
                    act.activation(h1T[:, c, :], late_ps[(ZB + KC + c) % 2][:, :], ACT.Relu,
                                   bias=b1_sb[:, c:c + 1]).then_inc(h1_ready, 1)

            def relu2(s):
                for c in range(C2):
                    act.wait_ge(h2_summed, C2 * s + c + 1)
                    act.activation(h2T[:, c, :], late_ps[(ZB + KC + C1 + c) % 2][:, :], ACT.Relu,
                                   bias=b2_sb[:, c:c + 1]).then_inc(h2_ready, 1)

            def store(s):
                act.wait_ge(y_summed, s + 1)
                if not first(s):
                    act.wait_ge(y_stored, 16 * s)
                act.copy(y_sb[0:1, :].rearrange("a (g j) -> a j g", j=J),
                         late_ps[(ZB + KC + C1 + C2) % 2][0:1, :].rearrange("a (j g) -> a j g", j=J),
                         ).then_inc(y_ready, 1)
                act.wait_ge(y_ready, s + 1)
                act.dma_start(y[bass.ds(s * BLOCK, BLOCK), :].rearrange("n a -> a n"),
                              y_sb[0:1, :]).then_inc(y_stored, 16)

            def body(s):
                for half in range(2):
                    if not (first(s) and half == 0):
                        act.wait_ge(dotted, UNITS * HT * (2 * s + half))
                    for o in range(O_FIRST):
                        copy_one_hot(s, half, o)
                    copy_turned(s, half * HT)
                    for o in range(O_FIRST, O):
                        copy_one_hot(s, half, o)
                    copy_turned(s, half * HT + 1)
                    if not first(s):
                        if half == 0:
                            copy_flat(s - 1)
                        else:
                            relu2(s - 1)
                    if first(s) and half == 0:
                        act.wait_ge(low_ready, O)
                    copy_gram(s, half * HT)
                    copy_gram(s, half * HT + 1)
                    if not first(s):
                        if half == 0:
                            relu1(s - 1)
                        else:
                            store(s - 1)
                if first(s):
                    act.wait_ge(weights_loaded, 16 * (KC + 4))

            for o in range(STAGES):
                load_table(o)
            for o in range(O):
                split_high(o)
                if o >= 1 and o - 1 + STAGES < O:
                    act.wait_ge(low_ready, o)
                    load_table(o - 1 + STAGES)
            each_block(act, body)
            copy_flat(BLOCKS - 1)
            relu1(BLOCKS - 1)
            relu2(BLOCKS - 1)
            store(BLOCKS - 1)
            act.wait_ge(y_stored, 16 * BLOCKS)


def kernel(**inputs):
    import numpy as np
    import concourse.bacc as bacc
    from concourse.bass_utils import run_bass_kernel_spmd

    arrays = {name: np.ascontiguousarray(a) for name, a in inputs.items()}
    for name in ("b_top1", "b_top2", "W_top3"):
        arrays[name] = np.ascontiguousarray(arrays[name].reshape(-1, P).T)
    arrays["idsT"] = np.ascontiguousarray(arrays["ids"].T)
    nc = bacc.Bacc("TRN2", target_bir_lowering=False, num_devices=1)
    ap = {name: nc.dram_tensor(f"in_{name}", a.shape, mybir.dt.from_np(a.dtype), kind="ExternalInput").ap()
          for name, a in arrays.items()}
    feats = arrays["ids"].shape[1]
    y = nc.dram_tensor("out_y", (arrays["ids"].shape[0], 1), F32, kind="ExternalOutput").ap()
    dlrm_tower(nc, ap["dense_ctx"], ap["ids"], ap["idsT"], [ap[f"tbl_{f}"] for f in range(feats)], ap["W_top1"], ap["b_top1"],
               ap["W_top2"], ap["b_top2"], ap["W_top3"], y)
    r = run_bass_kernel_spmd(nc, [{f"in_{name}": a for name, a in arrays.items()}], core_ids=[0])
    return r.results[0]["out_y"]
```

```python
from contextlib import ExitStack

import concourse.bass as bass
from concourse import mybir

P = 128
F32 = mybir.dt.float32
F32R = mybir.dt.float32r
I32 = mybir.dt.int32
ALU = mybir.AluOpType
ACT = mybir.ActivationFunctionType
ONE_HOT = (4, 13, 18, 19, 21, 22, 23)
ROWS_PER_CHUNK = 125
DIRECT = 6


def feature_order(feats):
    return [f for f in range(feats) if f not in ONE_HOT] + list(ONE_HOT)


def input_order(feats, dense):
    order = feature_order(feats)
    rows = []
    for some in (range(DIRECT, feats), range(1, DIRECT)):
        for n in some:
            for m in range(n):
                a, b = sorted((order[m], order[n]))
                rows.append(b * (b - 1) // 2 + a)
    return rows + list(range(len(rows), len(rows) + dense))


def dlrm_tower(nc, dense, ids, idsT, tables, w1, b1, w2, b2, w3, y):
    B, FEATS = ids.shape
    D = tables[0].shape[1]
    DENSE = dense.shape[1]
    H1, H2 = w2.shape
    FLAT = w1.shape[0]
    PAIRS = FEATS * (FEATS - 1) // 2
    assert D == P and FLAT == PAIRS + DENSE

    TILE = P
    TT = 4
    BLOCK = TILE * TT
    BLOCKS = B // BLOCK
    ROWS = 32
    J = P // ROWS
    G = BLOCK // J
    GT = TILE // J
    N = FEATS - DIRECT
    XP = DIRECT * (DIRECT - 1) // 2
    MAIN = PAIRS - XP
    X_AT = P - ROWS
    PER_BANK = 4
    GATHERED = [f for f in range(FEATS) if f not in ONE_HOT]
    GF = len(GATHERED)
    QUADS = -(-GF // PER_BANK)
    HALF = BLOCK // 2
    HT = HALF // TILE
    O = len(ONE_HOT)
    R = ROWS_PER_CHUNK
    CHUNKS = [tables[f].shape[0] // R for f in ONE_HOT]
    MAXC = max(CHUNKS)
    GROUP = 2
    GROUPS = [c // GROUP for c in CHUNKS]
    GROUP_AT = [sum(GROUPS[:o]) for o in range(O + 1)]
    GH = GROUP_AT[O]
    SLOTS = 8
    ID_SLOTS = O
    STEPS = O + HT * QUADS
    STAGES = 4
    assert all(tables[f].shape[0] == R * c and c % GROUP == 0 for f, c in zip(ONE_HOT, CHUNKS))
    assert 2 * GH % SLOTS == 0
    UNIT = PER_BANK
    UNITS = GT // UNIT
    GRAM_BANKS = 3
    ZB = -(-N // PER_BANK)
    KC = -(-MAIN // P)
    MAIN_ROWS = [min(P, MAIN - k * P) for k in range(KC)]
    K_ROWS = MAIN_ROWS[:-1] + [X_AT + XP + DENSE]
    assert MAIN_ROWS[-1] <= X_AT and XP + DENSE <= ROWS and MAIN_ROWS[-1] >= X_AT - ROWS
    C1 = H1 // P
    C2 = H2 // P

    def quad(q):
        return range(q * PER_BANK, min(GF, (q + 1) * PER_BANK))

    X_QUADS = -(-DIRECT // PER_BANK)
    X_PAIRS = [(m, n) for n in range(1, DIRECT) for m in range(n)]
    PRODUCTS = 3
    assert XP % PRODUCTS == 0 and C2 <= KC - 1

    EMBT_BANKS = 3

    def tile_plan(t):
        mine = range(-(-O * t // HT), -(-O * (t + 1) // HT))
        plan = []
        for i, o in enumerate(mine):
            share = range(QUADS * i // len(mine), QUADS * (i + 1) // len(mine))
            plan += [("quad", t, q) for q in share] + [("one_hot", o)]
        return plan

    plans = [tile_plan(t) for t in range(HT)]
    last_plans = [[step for step in plan if step[0] == "quad"] for plan in plans]
    PREPARED = 3
    assert sum(map(len, plans)) == STEPS and O > PREPARED and O % ID_SLOTS == 0

    def same_bank(at, steps_before):
        if at >= EMBT_BANKS:
            return EMBT_BANKS
        return at + steps_before - max(k for k in range(steps_before) if k % EMBT_BANKS == at)

    BACK = [same_bank(at, 2 * STEPS) for at in range(EMBT_BANKS + 1)]
    assert BACK == [same_bank(at, O) for at in range(EMBT_BANKS + 1)]

    ctx = ExitStack()
    with ctx:
        def sb(name, shape, dt=F32):
            return ctx.enter_context(nc.sbuf_tensor(name, shape, dt))

        def ps(name, shape):
            return ctx.enter_context(nc.psum_tensor(name, shape, F32))

        def sem(name):
            return ctx.enter_context(nc.semaphore(name))

        idx = sb("idx", [P, TT, FEATS], I32)
        extra = sb("extra", [P, TT, XP + DENSE])
        products = sb("products", [P, PRODUCTS, D])
        emb = sb("emb", [P, 2, GF, D])
        tbl_space = sb("tbl_space", [P, 2, sum(CHUNKS), D], F32R)
        ids_rows = sb("ids_rows", [R, ID_SLOTS, HALF], I32)
        one_hot = sb("one_hot", [R, SLOTS, GROUP, HALF], F32R)
        row_i = sb("row_i", [R, 1], I32)
        minus_row = sb("minus_row", [R, 1])
        embT = sb("embT", [P, TT, TILE, ROWS])
        gram = sb("gram", [P, N, G])
        flatT = sb("flatT", [P, KC, BLOCK])
        h1T = sb("h1T", [P, C1, BLOCK])
        y_sb = sb("y_sb", [1, BLOCK])
        w1_sb = sb("w1_sb", [P, KC, H1])
        w2_sb = sb("w2_sb", [P, C1, H2])
        w3_sb = sb("w3_sb", [P, C2])
        b1_sb = sb("b1_sb", [P, C1])
        b2_sb = sb("b2_sb", [P, C2])
        ident = sb("ident", [P, P])

        flat = h1T[:, :, :].rearrange("p c n -> p (c n)")[:, 0:J * MAIN].rearrange("p (j k) -> p j k", j=J)
        h2T = flatT
        tbl_parts = tbl_space[0:R, :, :, :]

        space = tbl_space[:, :, :, :].rearrange("p a c d -> p (a c d)")
        sizes = [KC * H1, C1 * H2, KC * BLOCK, C1 * BLOCK]
        assert 2 * sum(sizes) <= 2 * sum(CHUNKS) * D
        w1_parts, w2_parts, x_parts, h1_parts = (
            space[:, 2 * sum(sizes[:i]):2 * sum(sizes[:i + 1])].rearrange("p (a k n) -> p a k n", a=2, k=k)
            for i, k in enumerate((KC, C1, KC, C1)))
        embT_feats = embT[:, :, :, :].rearrange("p t c f -> p t f c")

        gram_flat = gram[0:R, :, :].rearrange("p n g -> p (n g)")
        stage = [gram_flat[:, 0:MAXC * D], gram_flat[:, MAXC * D:2 * MAXC * D],
                 h1T[0:R, :, :].rearrange("p c n -> p (c n)")[:, 0:MAXC * D],
                 flatT[0:R, :, :].rearrange("p c n -> p (c n)")[:, 0:MAXC * D]]
        part_at = [sum(CHUNKS[:o]) for o in range(O)]

        embT_ps = [ps(f"embT_ps{i}", [P, 512]) for i in range(EMBT_BANKS)]
        gram_ps = [ps(f"gram_ps{i}", [P, 512]) for i in range(GRAM_BANKS)]
        late_ps = [ps(f"late_ps{i}", [P, 512]) for i in range(2)]
        end_z_ps = embT_ps + gram_ps
        end_flat_ps = [late_ps[1], late_ps[0], embT_ps[0]]
        end_h1_ps = gram_ps + [embT_ps[1]]
        end_h2_ps = [embT_ps[2], late_ps[1]]
        end_y_ps = late_ps[0]
        assert ZB <= len(end_z_ps) and KC <= len(end_flat_ps) and C1 <= len(end_h1_ps) and C2 <= len(end_h2_ps)
        END_Z_OF_ACT = (1, 4)
        WHOLE = [(slice(0, P), slice(0, KC - 1)), (slice(0, K_ROWS[-1]), slice(KC - 1, KC))]

        ident_zeroed = sem("ident_zeroed")
        ident_ready = sem("ident_ready")
        pad_zeroed = sem("pad_zeroed")
        weights_loaded = sem("weights_loaded")
        idx_loaded = [sem(f"idx_loaded{t}") for t in range(TT)]
        gathered = [[sem(f"gathered{b}_{q}") for q in range(QUADS)] for b in range(2)]
        gather_allowed = sem("gather_allowed")
        turned = sem("turned")
        row_dotted = sem("row_dotted")
        w1_gap_zeroed = sem("w1_gap_zeroed")
        flatT_gap_zeroed = sem("flatT_gap_zeroed")
        extra_turned = sem("extra_turned")
        extra_ready = sem("extra_ready")
        rows_numbered = sem("rows_numbered")
        minus_row_ready = sem("minus_row_ready")
        ids_relative = sem("ids_relative")
        staged = [sem(f"staged{i}") for i in range(STAGES)]
        high_ready = sem("high_ready")
        low_ready = sem("low_ready")
        ids_loaded = [sem(f"ids_loaded{i}") for i in range(ID_SLOTS)]
        one_hot_built = sem("one_hot_built")
        one_hot_used = sem("one_hot_used")
        embT_ready = sem("embT_ready")
        dotted = sem("dotted")
        gram_ready = sem("gram_ready")
        z_turned = sem("z_turned")
        flat_ready = sem("flat_ready")
        dense_loaded = sem("dense_loaded")
        flat_turned = sem("flat_turned")
        flatT_ready = sem("flatT_ready")
        h1_summed = sem("h1_summed")
        h1_ready = sem("h1_ready")
        h2_summed = sem("h2_summed")
        h2_ready = sem("h2_ready")
        y_summed = sem("y_summed")
        y_ready = sem("y_ready")
        y_stored = sem("y_stored")
        weights_high = sem("weights_high")
        weights_low = sem("weights_low")
        extra_high = sem("extra_high")
        act_flat_ready = sem("act_flat_ready")
        x_high = sem("x_high")
        x_low = sem("x_low")
        h1_high = sem("h1_high")
        h1_low = sem("h1_low")

        block = ctx.enter_context(nc.Block())

        def each_block(eng, body):
            body(0)
            with eng.Fori(1, BLOCKS - 1) as s:
                body(s)
            body(BLOCKS - 1)

        def last(s):
            return isinstance(s, int) and s == BLOCKS - 1

        def alone(s, half):
            return last(s) and half == 1

        def steps(s, half, t):
            mine = last_plans if alone(s, half) else plans
            first_at = STEPS * half + sum(len(plan) for plan in mine[:t])
            for at, step in enumerate(mine[t], first_at):
                before = O + 2 * STEPS * s + at
                yield step[0], step[1:], at % EMBT_BANKS, before, before + 1 - BACK[min(at, EMBT_BANKS)]

        def copied(s, half, t):
            return [before for kind, _, _, before, _ in steps(s, half, t) if kind == "quad"][-1] + 1

        def z_after(o):
            return range(min(ZB, max(0, 2 * o - 1)), min(ZB, 2 * o + 1))

        def dots_to_flat(copy, bank, z):
            for i, n in enumerate(range(DIRECT + z * PER_BANK, DIRECT + min(N, (z + 1) * PER_BANK))):
                at = n * (n - 1) // 2 - XP
                done = copy(flat[:, :, at:at + n],
                            bank[:, i * P:(i + 1) * P].rearrange("p (j m) -> p j m", j=J)[:, :, 0:n])
            return done

        def to_order(rows):
            return rows.rearrange("r (j t g) -> r t g j", j=J, t=TT)

        def from_samples(rows):
            return rows.rearrange("r (t g j) -> r t g j", j=J, t=TT)

        def following(s, half):
            return (s, 1) if half == 0 else (s + 1, 0)

        def first(s):
            return isinstance(s, int) and s == 0

        @block.sync
        def _(sp):
            def load_idx(s, t):
                if not first(s):
                    sp.wait_ge(turned, QUADS * (TT * (s - 1) + t + 1))
                sp.dma_start(idx[:, t, :], ids[bass.ds(s * BLOCK + t * TILE, TILE), :]).then_inc(idx_loaded[t], 16)

            def load_ids(s, half, some):
                for o in some:
                    f = ONE_HOT[o]
                    if not (first(s) and half == 0 and o < ID_SLOTS):
                        sp.wait_ge(one_hot_built, GH * (2 * s + half - (o < ID_SLOTS)) +
                                   GROUP_AT[(o - ID_SLOTS) % O + 1])
                    src = idsT[f:f + 1, bass.ds(s * BLOCK + half * HALF, HALF)].to_broadcast([R, HALF])
                    sp.dma_start(ids_rows[:, o % ID_SLOTS, :], src).then_inc(ids_loaded[o % ID_SLOTS], 16)

            def load_dense(s):
                if not first(s):
                    sp.wait_ge(extra_turned, s)
                src = dense[bass.ds(s * BLOCK, BLOCK), :].rearrange("(t p) f -> p t f", t=TT)
                sp.dma_start(extra[:, :, XP:XP + DENSE], src).then_inc(dense_loaded, 16)

            load_idx(0, 0)
            load_ids(0, 0, range(ID_SLOTS))
            for t in range(1, TT):
                load_idx(0, t)
            load_ids(0, 0, range(ID_SLOTS, O))
            sp.wait_ge(w1_gap_zeroed, 1)
            for k in range(KC):
                sp.dma_start(w1_sb[0:MAIN_ROWS[k], k, :], w1[k * P:k * P + MAIN_ROWS[k], :]).then_inc(weights_loaded, 16)
            sp.dma_start(w1_sb[X_AT:X_AT + XP + DENSE, KC - 1, :], w1[MAIN:FLAT, :]).then_inc(weights_loaded, 16)
            sp.dma_start(w2_sb[:, :, :], w2.rearrange("(k p) n -> p k n", p=P)).then_inc(weights_loaded, 16)
            sp.dma_start(w3_sb[:, :], w3).then_inc(weights_loaded, 16)
            sp.dma_start(b1_sb[:, :], b1).then_inc(weights_loaded, 16)
            sp.dma_start(b2_sb[:, :], b2).then_inc(weights_loaded, 16)
            load_dense(0)
            load_ids(0, 1, range(O))
            with sp.Fori(1, BLOCKS) as s:
                for half in range(2):
                    load_ids(s, half, range(PREPARED))
                    for t in range(half * HT, (half + 1) * HT):
                        load_idx(s, t)
                    if half == 1:
                        load_dense(s)
                    load_ids(s, half, range(PREPARED, O))

        @block.gpsimd
        def _(pool):
            pool.memset(ident[:, :], 0.0).then_inc(ident_zeroed, 1)
            pool.wait_ge(ident_zeroed, 1)
            pool.affine_select(out=ident[:, :], in_=ident[:, :], compare_op=ALU.not_equal, fill=1.0, base=0,
                               pattern=[[-1, P]], channel_multiplier=1).then_inc(ident_ready, 1)

            pool.iota(row_i[:, :], pattern=[[0, 1]], base=0, channel_multiplier=-1).then_inc(rows_numbered, 1)

            def gathers(s):
                for t in range(TT):
                    pool.wait_ge(idx_loaded[t], 16 * (s + 1))
                    for q in range(QUADS):
                        if not (first(s) and t < 2):
                            pool.wait_ge(turned, QUADS * (TT * s + t - 2) + q + 1)
                            if q < X_QUADS:
                                pool.wait_ge(row_dotted, XP * (TT * s + t - 1))
                        pool.sem_inc(gather_allowed, 1)
                        for f in quad(q):
                            pool.indirect_dma_start(
                                emb[:, t % 2, f, :], None, tables[GATHERED[f]][:, :],
                                bass.IndirectOffsetOnAxis(ap=idx[:, t, GATHERED[f]:GATHERED[f] + 1], axis=0),
                            ).then_inc(gathered[t % 2][q], 16)

            each_block(pool, gathers)

        @block.tensor
        def _(pe):
            pe.wait_ge(ident_ready, 1)
            pe.wait_ge(pad_zeroed, TT)

            def bank_free(done):
                if not (isinstance(done, int) and done <= 0):
                    pe.wait_ge(embT_ready, done)

            def read_one_hot(s, half, o, bank, done):
                bank_free(done)
                if first(s) and half == 0:
                    pe.wait_ge(low_ready, o + 1)
                for i in range(GROUPS[o]):
                    k = GROUP_AT[o] + i
                    pe.wait_ge(one_hot_built, GH * (2 * s + half) + k + 1)
                    for c in range(GROUP):
                        chunk = i * GROUP + c
                        for part in range(2):
                            mm = pe.matmul(embT_ps[bank][:, 0:HALF], tbl_parts[:, part, part_at[o] + chunk, :],
                                           one_hot[:, (half * GH + k) % SLOTS, c, :],
                                           start=(chunk == 0 and part == 0),
                                           stop=(chunk == CHUNKS[o] - 1 and part == 1))
                    mm.then_inc(one_hot_used, 1)

            def turn(s, t, q, bank, done):
                pe.wait_ge(gathered[t % 2][q], 16 * len(quad(q)) * (2 * s + t // 2 + 1))
                bank_free(done)
                for i in range(len(quad(q))):
                    mm = pe.transpose(embT_ps[bank][:, i * P:(i + 1) * P], emb[:, t % 2, q * PER_BANK + i, :],
                                      ident[:, :])
                mm.then_inc(turned, 1)

            def dots(s, t):
                for u in range(UNITS):
                    same = u - GRAM_BANKS if u >= GRAM_BANKS else (UNITS - 1 - u) // GRAM_BANKS * GRAM_BANKS + u - UNITS
                    if not (first(s) and t == 0 and same < 0):
                        pe.wait_ge(gram_ready, UNITS * (TT * s + t) + same + 1)
                    for i in range(UNIT):
                        c = (u * UNIT + i) * J
                        o = gram_ps[u % GRAM_BANKS][:, i * J * N:(i + 1) * J * N]
                        mm = pe.matmul(o, embT[:, t, c:c + J, :], embT[:, t, c:c + J, DIRECT:FEATS],
                                         start=True, stop=True)
                    mm.then_inc(dotted, 1)

            def turn_extra(s):
                pe.wait_ge(row_dotted, XP * TT * (s + 1))
                pe.wait_ge(dense_loaded, 16 * (s + 1))
                if not first(s):
                    pe.wait_ge(*(h2_ready, C2 * s) if last(s) else (h1_ready, C1 * s))
                for t in range(TT):
                    mm = pe.transpose(late_ps[1][0:XP + DENSE, t * P:(t + 1) * P], extra[:, t, :], ident[:, :])
                mm.then_inc(extra_turned, 1)

            def turn_dots(s, z):
                if z == 0:
                    pe.wait_ge(gram_ready, UNITS * TT * (s + 1))
                    pe.wait_ge(extra_ready, s + 1)
                    if not first(s):
                        pe.wait_ge(y_ready, s)
                elif z >= 2:
                    pe.wait_ge(flat_ready, ZB * s + z - 1)
                for i, n in enumerate(range(z * PER_BANK, min(N, (z + 1) * PER_BANK))):
                    mm = pe.transpose(late_ps[(1 + z) % 2][:, i * P:(i + 1) * P], gram[:, n, :], ident[:, :])
                mm.then_inc(z_turned, 1)

            def turn_flat(s):
                pe.wait_ge(flat_ready, ZB * (s + 1))
                for k in range(KC):
                    if k >= 2:
                        pe.wait_ge(flatT_ready, KC * s + k - 1)
                    for j in range(J):
                        mm = pe.transpose(late_ps[(1 + ZB + k) % 2][0:MAIN_ROWS[k], j * P:(j + 1) * P],
                                          flat[:, j, k * P:k * P + MAIN_ROWS[k]], ident[:, :])
                    mm.then_inc(flat_turned, 1)

            def layer1(s):
                pe.wait_ge(flatT_ready, KC * (s + 1))
                pe.wait_ge(extra_ready, s + 1)
                pe.wait_ge(flatT_gap_zeroed, 1)
                for c in range(C1):
                    if c >= 2:
                        pe.wait_ge(h1_ready, C1 * s + c - 1)
                    for k in range(KC):
                        rows = K_ROWS[k]
                        mm = pe.matmul(late_ps[(1 + ZB + KC + c) % 2][:, :], w1_sb[0:rows, k, c * P:(c + 1) * P],
                                       flatT[0:rows, k, :], start=(k == 0), stop=(k == KC - 1))
                    mm.then_inc(h1_summed, 1)

            def layer2(s):
                pe.wait_ge(h1_ready, C1 * (s + 1))
                for c in range(C2):
                    if c == 1:
                        pe.wait_ge(extra_ready, s + 2)
                    for k in range(C1):
                        mm = pe.matmul(late_ps[(1 + ZB + KC + C1 + c) % 2][:, :], w2_sb[:, k, c * P:(c + 1) * P],
                                         h1T[:, k, :], start=(k == 0), stop=(k == C1 - 1))
                    mm.then_inc(h2_summed, 1)

            def layer3(s):
                pe.wait_ge(h2_ready, C2 * (s + 1))
                for k in range(C2):
                    mm = pe.matmul(late_ps[(1 + ZB + KC + C1 + C2) % 2][0:1, :], w3_sb[:, k:k + 1], h2T[:, k, :],
                                     start=(k == 0), stop=(k == C2 - 1))
                mm.then_inc(y_summed, 1)

            def split_products(out, lhs, rhs, cols, rows, high_waits, low_wait):
                n = len(rows)
                terms = [(0, 0, k) for k in range(n)] + [(1, 0, k) for k in range(n)] + [(0, 1, k) for k in range(n)]
                for i, (a, b, k) in enumerate(terms):
                    if i < n and high_waits:
                        pe.wait_ge(*high_waits[k])
                    if i == 2 * n and low_wait:
                        pe.wait_ge(*low_wait)
                    mm = pe.matmul(out[:, :], lhs[0:rows[k], a, k, cols], rhs[0:rows[k], b, k, :],
                                   start=(i == 0), stop=(i == len(terms) - 1))
                return mm

            def split_layer2(s, banks):
                done = C1 * (s - (BLOCKS - 2))
                for c in range(C2):
                    split_products(banks[c], w2_parts, h1_parts, slice(c * P, (c + 1) * P), [P] * C1,
                                   c == 0 and [(h1_high, done + k + 1) for k in range(C1)],
                                   c == 0 and (h1_low, done + C1)).then_inc(h2_summed, 1)

            def end():
                s = BLOCKS - 1
                pe.wait_ge(gram_ready, UNITS * TT * BLOCKS)
                for z in range(ZB):
                    for i, n in enumerate(range(z * PER_BANK, min(N, (z + 1) * PER_BANK))):
                        mm = pe.transpose(end_z_ps[z][:, i * P:(i + 1) * P], gram[:, n, :], ident[:, :])
                    mm.then_inc(z_turned, 1)
                pe.wait_ge(flat_ready, ZB * BLOCKS - len(END_Z_OF_ACT))
                pe.wait_ge(act_flat_ready, len(END_Z_OF_ACT))
                pe.wait_ge(extra_ready, BLOCKS)
                pe.wait_ge(y_ready, s)
                for k in range(KC):
                    for j in range(J):
                        mm = pe.transpose(end_flat_ps[k][0:MAIN_ROWS[k], j * P:(j + 1) * P],
                                          flat[:, j, k * P:k * P + MAIN_ROWS[k]], ident[:, :])
                    mm.then_inc(flat_turned, 1)
                pe.wait_ge(weights_low, len(WHOLE) + 1)
                for c in range(C1):
                    split_products(end_h1_ps[c], w1_parts, x_parts, slice(c * P, (c + 1) * P), K_ROWS,
                                   c == 0 and [(x_high, k + 1) for k in range(KC)],
                                   c == 0 and (x_low, KC)).then_inc(h1_summed, 1)
                split_layer2(s, end_h2_ps)
                for k in range(C2):
                    pe.wait_ge(h2_ready, C2 * s + k + 1)
                    mm = pe.matmul(end_y_ps[0:1, :], w3_sb[:, k:k + 1], h2T[:, k, :],
                                   start=(k == 0), stop=(k == C2 - 1))
                mm.then_inc(y_summed, 1)

            def tile(s, half, t):
                for kind, what, bank, _, done in steps(s, half, t):
                    if kind == "quad":
                        turn(s, half * HT + what[0], what[1], bank, done)
                        if alone(s, half) and t == 1 and what[1] == QUADS - 2:
                            layer3(s - 1)
                        continue
                    o = what[0]
                    read_one_hot(*following(s, half), o, bank, done)
                    if half == 0 and not first(s):
                        for z in z_after(o):
                            turn_dots(s - 1, z)
                        if o == O - 2:
                            turn_flat(s - 1)
                if half == 0 and t == 1 and not first(s):
                    layer1(s - 1)
                if half == 1 and t == 1:
                    turn_extra(s)
                    if not first(s) and not last(s):
                        layer2(s - 1)
                pe.wait_ge(embT_ready, copied(s, half, t))
                dots(s, half * HT + t)
                if alone(s, half) and t == 0:
                    pe.wait_ge(h1_ready, C1 * s)
                    pe.wait_ge(weights_low, len(WHOLE) + 1)
                    split_layer2(s - 1, [late_ps[(1 + ZB + KC + C1 + c) % 2] for c in range(C2)])

            def body(s):
                for half in range(2):
                    for t in range(HT):
                        tile(s, half, t)
                if first(s):
                    pe.wait_ge(weights_loaded, 16 * (KC + 5))
                elif not last(s):
                    layer3(s - 1)

            for o in range(O):
                read_one_hot(0, 0, o, o % EMBT_BANKS, o - EMBT_BANKS + 1)
            each_block(pe, body)
            end()

        @block.vector
        def _(dve):
            dve.memset(w1_sb[X_AT - ROWS:X_AT, KC - 1, :], 0.0).then_inc(w1_gap_zeroed, 1)
            for t in range(TT):
                dve.memset(embT[:, t, :, FEATS:ROWS], 0.0).then_inc(pad_zeroed, 1)

            def split_low(o):
                at = slice(part_at[o], part_at[o] + CHUNKS[o])
                raw = stage[o % STAGES][:, 0:CHUNKS[o] * D].rearrange("p (c d) -> p c d", d=D)
                dve.wait_ge(high_ready, o + 1)
                dve.tensor_tensor(tbl_parts[:, 1, at, :], raw, tbl_parts[:, 0, at, :].bitcast(F32),
                                  ALU.subtract).then_inc(low_ready, 1)

            def build(s, half, o):
                dve.wait_ge(ids_relative, O * (2 * s + half) + o + 1)
                for i in range(GROUPS[o]):
                    k = GROUP_AT[o] + i
                    if not (first(s) and half == 0 and k < SLOTS):
                        dve.wait_ge(one_hot_used, GH * (2 * s + half) + k - SLOTS + 1)
                    for c in range(GROUP):
                        chunk = i * GROUP + c
                        done = dve.tensor_scalar(one_hot[:, (half * GH + k) % SLOTS, c, :],
                                                 ids_rows[:, o % ID_SLOTS, :].bitcast(F32),
                                                 float(R * chunk), None, ALU.is_equal)
                    done.then_inc(one_hot_built, 1)

            def copy_dots(s, z):
                if z == 0 and not first(s):
                    dve.wait_ge(h2_summed, C2 * s)
                dve.wait_ge(z_turned, ZB * s + z + 1)
                done = dots_to_flat(dve.tensor_copy, late_ps[(1 + z) % 2], z)
                done.then_inc(flat_ready, 1)

            def dot_rows(s, t):
                for q in range(X_QUADS):
                    dve.wait_ge(gathered[t % 2][q], 16 * len(quad(q)) * (2 * s + t // 2 + 1))
                if t == 0 and not first(s):
                    dve.wait_ge(extra_turned, s)
                for i, (m, n) in enumerate(X_PAIRS):
                    if not (first(s) and t == 0 and i < PRODUCTS):
                        dve.wait_ge(row_dotted, XP * (TT * s + t) + i - PRODUCTS + 1)
                    dve.tensor_tensor_reduce(
                        out=products[:, i % PRODUCTS, :], in0=emb[:, t % 2, m, :], in1=emb[:, t % 2, n, :],
                        scale=1.0, scalar=0.0, op0=ALU.mult, op1=ALU.add,
                        accum_out=extra[:, t, i:i + 1]).then_inc(row_dotted, 1)

            def tile(s, half, t):
                for kind, what, _, _, _ in steps(s, half, t):
                    if kind == "one_hot":
                        o = what[0]
                        build(*following(s, half), o)
                        if half == 0 and not first(s) and o >= 1:
                            for z in z_after(o - 1):
                                copy_dots(s - 1, z)
                    if kind == "quad" and what[1] == X_QUADS - 1:
                        dot_rows(s, half * HT + t)

            def body(s):
                for half in range(2):
                    for t in range(HT):
                        tile(s, half, t)
                    if last(s) and half == 0:
                        weight_lows()
                        h1_lows(s - 1)

            def low(part, whole, high, done):
                dve.tensor_tensor(part, whole, high.bitcast(F32), ALU.subtract).then_inc(done, 1)

            def h1_lows(s):
                for c in range(C1):
                    dve.wait_ge(h1_ready, C1 * s + c + 1)
                    low(h1_parts[:, 1, c, :], h1T[:, c, :], h1_parts[:, 0, c, :], h1_low)

            def weight_lows():
                for i, (rows, ks) in enumerate(WHOLE):
                    dve.wait_ge(weights_high, i + 1)
                    low(w1_parts[rows, 1, ks, :], w1_sb[rows, ks, :], w1_parts[rows, 0, ks, :], weights_low)
                dve.wait_ge(weights_high, len(WHOLE) + 1)
                low(w2_parts[:, 1, :, :], w2_sb[:, :, :], w2_parts[:, 0, :, :], weights_low)

            def end():
                dve.wait_ge(extra_high, 1)
                low(to_order(x_parts[X_AT:K_ROWS[-1], 1, KC - 1, :]), from_samples(late_ps[1][0:XP + DENSE, :]),
                    to_order(x_parts[X_AT:K_ROWS[-1], 0, KC - 1, :]), extra_ready)
                dve.wait_ge(h2_summed, C2 * (BLOCKS - 1))
                for z in range(ZB):
                    if z not in END_Z_OF_ACT:
                        dve.wait_ge(z_turned, ZB * (BLOCKS - 1) + z + 1)
                        dots_to_flat(dve.tensor_copy, end_z_ps[z], z).then_inc(flat_ready, 1)
                for k in range(KC):
                    dve.wait_ge(x_high, k + 1)
                    rows = slice(0, MAIN_ROWS[k])
                    low(x_parts[rows, 1, k, :], end_flat_ps[k][rows, :], x_parts[rows, 0, k, :], x_low)
                h1_lows(BLOCKS - 1)

            for o in range(O):
                if o == 0:
                    build(0, 0, o)
                split_low(o)
                if o > 0:
                    build(0, 0, o)
            dve.memset(flatT[X_AT - ROWS:X_AT, KC - 1, :], 0.0).then_inc(flatT_gap_zeroed, 1)
            each_block(dve, body)
            end()

        @block.scalar
        def _(act):
            SPLIT_AHEAD = 2

            def load_table(o):
                f = ONE_HOT[o]
                act.dma_start(stage[o % STAGES][:, 0:CHUNKS[o] * D].rearrange("p (c d) -> p c d", d=D),
                              tables[f].rearrange("(c p) d -> p c d", p=R)).then_inc(staged[o % STAGES], 16)

            def split_high(o):
                raw = stage[o % STAGES][:, 0:CHUNKS[o] * D].rearrange("p (c d) -> p c d", d=D)
                act.wait_ge(staged[o % STAGES], 16 * (o // STAGES + 1))
                act.copy(tbl_parts[:, 0, part_at[o]:part_at[o] + CHUNKS[o], :], raw).then_inc(high_ready, 1)

            def prepare(s, half, o):
                act.wait_ge(ids_loaded[o % ID_SLOTS], 16 * (O // ID_SLOTS * (2 * s + half) + o // ID_SLOTS + 1))
                ids_of = ids_rows[:, o % ID_SLOTS, :]
                act.activation(ids_of.bitcast(F32), ids_of, ACT.Identity, bias=minus_row[:, :]).then_inc(ids_relative, 1)

            def prepare_after(s, half, o):
                if o + PREPARED < O:
                    prepare(s, half, o + PREPARED)
                elif not alone(s, half):
                    prepare(*following(s, half), o + PREPARED - O)

            def copy_one_hot(s, half, o, bank):
                act.wait_ge(one_hot_used, GH * (2 * s + half) + GROUP_AT[o + 1])
                act.copy(embT_feats[:, half * HT:(half + 1) * HT, GF + o, :],
                         embT_ps[bank][:, 0:HALF].rearrange("p (t c) -> p t c", t=HT)).then_inc(embT_ready, 1)

            def copy_turned(s, t, q, bank):
                n = len(quad(q))
                act.wait_ge(turned, QUADS * (TT * s + t) + q + 1)
                act.copy(embT_feats[:, t, quad(q)[0]:quad(q)[0] + n, :],
                         embT_ps[bank][:, 0:n * P].rearrange("p (f c) -> p f c", f=n)).then_inc(embT_ready, 1)

            def copy_gram(s, t):
                if t == 0 and not first(s):
                    act.wait_ge(z_turned, ZB * s)
                for u in range(UNITS):
                    act.wait_ge(dotted, UNITS * (TT * s + t) + u + 1)
                    g = t * GT + u * UNIT
                    for j in range(J):
                        rows = slice(j * ROWS, (j + 1) * ROWS)
                        src = gram_ps[u % GRAM_BANKS][rows, 0:UNIT * J * N].rearrange(
                            "p (g j n) -> p g j n", g=UNIT, j=J)[:, :, j, :]
                        dst = gram[rows, :, g:g + UNIT].rearrange("p n g -> p g n")
                        done = act.copy(dst, src)
                    done.then_inc(gram_ready, 1)

            def copy_extra(s):
                act.wait_ge(extra_turned, s + 1)
                if last(s):
                    act.copy(to_order(x_parts[X_AT:K_ROWS[-1], 0, KC - 1, :]),
                             from_samples(late_ps[1][0:XP + DENSE, :])).then_inc(extra_high, 1)
                else:
                    act.copy(to_order(flatT[X_AT:K_ROWS[-1], KC - 1, :]),
                             from_samples(late_ps[1][0:XP + DENSE, :])).then_inc(extra_ready, 1)

            def copy_flat(s):
                for k in range(KC):
                    act.wait_ge(flat_turned, KC * s + k + 1)
                    if k == KC - 1:
                        act.wait_ge(flatT_gap_zeroed, 1)
                    act.copy(flatT[0:MAIN_ROWS[k], k, :],
                             late_ps[(1 + ZB + k) % 2][0:MAIN_ROWS[k], :]).then_inc(flatT_ready, 1)

            def relu1(s):
                for c in range(C1):
                    act.wait_ge(h1_summed, C1 * s + c + 1)
                    act.activation(h1T[:, c, :], late_ps[(1 + ZB + KC + c) % 2][:, :], ACT.Relu,
                                   bias=b1_sb[:, c:c + 1]).then_inc(h1_ready, 1)

            def relu2(s):
                for c in range(C2):
                    act.wait_ge(h2_summed, C2 * s + c + 1)
                    act.activation(h2T[:, c, :], late_ps[(1 + ZB + KC + C1 + c) % 2][:, :], ACT.Relu,
                                   bias=b2_sb[:, c:c + 1]).then_inc(h2_ready, 1)

            def split_weights():
                for rows, ks in WHOLE:
                    act.copy(w1_parts[rows, 0, ks, :], w1_sb[rows, ks, :]).then_inc(weights_high, 1)
                act.copy(w2_parts[:, 0, :, :], w2_sb[:, :, :]).then_inc(weights_high, 1)
                act.wait_ge(flatT_ready, KC * (BLOCKS - 1))
                for part in range(2):
                    gap = slice(X_AT - ROWS, X_AT)
                    act.copy(x_parts[gap, part, KC - 1, :], flatT[gap, KC - 1, :])

            def split_relu1(s, banks):
                for c in range(C1):
                    act.wait_ge(h1_summed, C1 * s + c + 1)
                    act.activation(h1_parts[:, 0, c, :], banks[c][:, :], ACT.Relu,
                                   bias=b1_sb[:, c:c + 1]).then_inc(h1_high, 1)
                    act.activation(h1T[:, c, :], banks[c][:, :], ACT.Relu,
                                   bias=b1_sb[:, c:c + 1]).then_inc(h1_ready, 1)

            def end():
                s = BLOCKS - 1
                act.wait_ge(h2_summed, C2 * s)
                for z in END_Z_OF_ACT:
                    act.wait_ge(z_turned, ZB * s + z + 1)
                    dots_to_flat(act.copy, end_z_ps[z], z).then_inc(act_flat_ready, 1)
                for k in range(KC):
                    act.wait_ge(flat_turned, KC * s + k + 1)
                    rows = slice(0, MAIN_ROWS[k])
                    act.copy(x_parts[rows, 0, k, :], end_flat_ps[k][rows, :]).then_inc(x_high, 1)
                split_relu1(s, end_h1_ps)
                for c in range(C2):
                    act.wait_ge(h2_summed, C2 * s + c + 1)
                    act.activation(h2T[:, c, :], end_h2_ps[c][:, :], ACT.Relu,
                                   bias=b2_sb[:, c:c + 1]).then_inc(h2_ready, 1)
                store(s, end_y_ps)

            def store(s, bank):
                act.wait_ge(y_summed, s + 1)
                if not first(s):
                    act.wait_ge(y_stored, 16 * s)
                act.copy(y_sb[0:1, :].rearrange("a (g j) -> a j g", j=J),
                         bank[0:1, :].rearrange("a (j g) -> a j g", j=J),
                         ).then_inc(y_ready, 1)
                act.wait_ge(y_ready, s + 1)
                act.dma_start(y[bass.ds(s * BLOCK, BLOCK), :].rearrange("n a -> a n"),
                              y_sb[0:1, :]).then_inc(y_stored, 16)

            def tile(s, half, t):
                for kind, what, bank, _, _ in steps(s, half, t):
                    if kind == "quad":
                        copy_turned(s, half * HT + what[0], what[1], bank)
                        if alone(s, half) and t == 1 and what[1] == QUADS - 1:
                            store(s - 1, late_ps[(1 + ZB + KC + C1 + C2) % 2])
                        continue
                    o = what[0]
                    copy_one_hot(*following(s, half), o, bank)
                    prepare_after(*following(s, half), o)
                    if half == 0 and not first(s) and o == O - 2:
                        copy_flat(s - 1)
                if half == 0 and t == 1 and not first(s):
                    if last(s):
                        split_weights()
                        split_relu1(s - 1, [late_ps[(1 + ZB + KC + c) % 2] for c in range(C1)])
                    else:
                        relu1(s - 1)
                if half == 1 and t == 1:
                    copy_extra(s)
                    if not first(s) and not last(s):
                        relu2(s - 1)
                copy_gram(s, half * HT + t)
                if alone(s, half) and t == 0:
                    relu2(s - 1)

            def body(s):
                for half in range(2):
                    if not (first(s) and half == 0):
                        act.wait_ge(dotted, UNITS * HT * (2 * s + half))
                    for t in range(HT):
                        tile(s, half, t)
                if first(s):
                    act.wait_ge(weights_loaded, 16 * (KC + 5))
                elif not last(s):
                    store(s - 1, late_ps[(1 + ZB + KC + C1 + C2) % 2])

            for o in range(STAGES):
                load_table(o)
            act.wait_ge(rows_numbered, 1)
            act.copy(minus_row[:, :], row_i[:, :]).then_inc(minus_row_ready, 1)
            act.wait_ge(minus_row_ready, 1)
            for o in range(SPLIT_AHEAD):
                split_high(o)
                prepare(0, 0, o)
            for o in range(SPLIT_AHEAD, PREPARED):
                prepare(0, 0, o)
            for o in range(O):
                if o + SPLIT_AHEAD < O:
                    split_high(o + SPLIT_AHEAD)
                copy_one_hot(0, 0, o, o % EMBT_BANKS)
                prepare_after(0, 0, o)
                if o + STAGES < O:
                    load_table(o + STAGES)
            act.wait_ge(low_ready, O)
            each_block(act, body)
            end()
            act.wait_ge(y_stored, 16 * BLOCKS)


def kernel(**inputs):
    import numpy as np
    import concourse.bacc as bacc
    from concourse.bass_utils import run_bass_kernel_spmd

    arrays = {name: np.ascontiguousarray(a) for name, a in inputs.items()}
    for name in ("b_top1", "b_top2", "W_top3"):
        arrays[name] = np.ascontiguousarray(arrays[name].reshape(-1, P).T)
    order = input_order(arrays["ids"].shape[1], arrays["dense_ctx"].shape[1])
    arrays["W_top1"] = np.ascontiguousarray(arrays["W_top1"][order])
    arrays["idsT"] = np.ascontiguousarray(arrays["ids"].T)
    nc = bacc.Bacc("TRN2", target_bir_lowering=False, num_devices=1)
    ap = {name: nc.dram_tensor(f"in_{name}", a.shape, mybir.dt.from_np(a.dtype), kind="ExternalInput").ap()
          for name, a in arrays.items()}
    feats = arrays["ids"].shape[1]
    y = nc.dram_tensor("out_y", (arrays["ids"].shape[0], 1), F32, kind="ExternalOutput").ap()
    dlrm_tower(nc, ap["dense_ctx"], ap["ids"], ap["idsT"], [ap[f"tbl_{f}"] for f in range(feats)], ap["W_top1"], ap["b_top1"],
               ap["W_top2"], ap["b_top2"], ap["W_top3"], y)
    r = run_bass_kernel_spmd(nc, [{f"in_{name}": a for name, a in arrays.items()}], core_ids=[0])
    return r.results[0]["out_y"]
```
